# Optimizing a Trainium2 kernel written in Bass

```python
import numpy as np
import jax
import jax.numpy as jnp

def _softmax(x, axis=-1):
    return jax.nn.softmax(x, axis=axis)

def _gelu(x):
    return jax.nn.gelu(x, approximate=True)

def _silu(x):
    return jax.nn.silu(x)

def _sigmoid(x):
    return jax.nn.sigmoid(x)

def _layernorm(x, axis=-1, eps=1e-05):
    m = jnp.mean(x, axis=axis, keepdims=True)
    v = jnp.var(x, axis=axis, keepdims=True)
    return (x - m) / jnp.sqrt(v + eps)

def _scatter_add(tgt, idx, src, axis=0):
    return tgt.at[idx].add(src)

def _segment_sum(src, seg, n):
    return jax.ops.segment_sum(src, seg, n)
kernel_name = 'mk_dlrm_tower_d1_rec_r8_d8a952'

def setup_inputs(seed: int=0):
    np.random.seed(seed)
    _w = jnp.asarray

    def _rec_inputs():
        import jax
        import jax.numpy as jnp
        _tk = jax.random.key(seed)
        ids = jnp.stack([jax.random.randint(jax.random.fold_in(_tk, 200 + f), (512,), 0, v, jnp.int32) for f, v in enumerate([1250, 12500, 12500, 1000, 1250, 1250, 1250, 1250, 125000, 12500, 1250, 1250, 12500, 1250, 12500, 1000, 1000, 12500, 12500, 1000, 12500, 1250, 1000, 1250, 1250, 1250])], axis=1)
        tbl_0 = 0.05 * jax.random.normal(jax.random.fold_in(_tk, 500 + 0), (1250, 128), jnp.float32)
        tbl_1 = 0.05 * jax.random.normal(jax.random.fold_in(_tk, 500 + 1), (12500, 128), jnp.float32)
        tbl_2 = 0.05 * jax.random.normal(jax.random.fold_in(_tk, 500 + 2), (12500, 128), jnp.float32)
        tbl_3 = 0.05 * jax.random.normal(jax.random.fold_in(_tk, 500 + 3), (1000, 128), jnp.float32)
        tbl_4 = 0.05 * jax.random.normal(jax.random.fold_in(_tk, 500 + 4), (1250, 128), jnp.float32)
        tbl_5 = 0.05 * jax.random.normal(jax.random.fold_in(_tk, 500 + 5), (1250, 128), jnp.float32)
        tbl_6 = 0.05 * jax.random.normal(jax.random.fold_in(_tk, 500 + 6), (1250, 128), jnp.float32)
        tbl_7 = 0.05 * jax.random.normal(jax.random.fold_in(_tk, 500 + 7), (1250, 128), jnp.float32)
        tbl_8 = 0.05 * jax.random.normal(jax.random.fold_in(_tk, 500 + 8), (125000, 128), jnp.float32)
        tbl_9 = 0.05 * jax.random.normal(jax.random.fold_in(_tk, 500 + 9), (12500, 128), jnp.float32)
        tbl_10 = 0.05 * jax.random.normal(jax.random.fold_in(_tk, 500 + 10), (1250, 128), jnp.float32)
        tbl_11 = 0.05 * jax.random.normal(jax.random.fold_in(_tk, 500 + 11), (1250, 128), jnp.float32)
        tbl_12 = 0.05 * jax.random.normal(jax.random.fold_in(_tk, 500 + 12), (12500, 128), jnp.float32)
        tbl_13 = 0.05 * jax.random.normal(jax.random.fold_in(_tk, 500 + 13), (1250, 128), jnp.float32)
        tbl_14 = 0.05 * jax.random.normal(jax.random.fold_in(_tk, 500 + 14), (12500, 128), jnp.float32)
        tbl_15 = 0.05 * jax.random.normal(jax.random.fold_in(_tk, 500 + 15), (1000, 128), jnp.float32)
        tbl_16 = 0.05 * jax.random.normal(jax.random.fold_in(_tk, 500 + 16), (1000, 128), jnp.float32)
        tbl_17 = 0.05 * jax.random.normal(jax.random.fold_in(_tk, 500 + 17), (12500, 128), jnp.float32)
        tbl_18 = 0.05 * jax.random.normal(jax.random.fold_in(_tk, 500 + 18), (12500, 128), jnp.float32)
        tbl_19 = 0.05 * jax.random.normal(jax.random.fold_in(_tk, 500 + 19), (1000, 128), jnp.float32)
        tbl_20 = 0.05 * jax.random.normal(jax.random.fold_in(_tk, 500 + 20), (12500, 128), jnp.float32)
        tbl_21 = 0.05 * jax.random.normal(jax.random.fold_in(_tk, 500 + 21), (1250, 128), jnp.float32)
        tbl_22 = 0.05 * jax.random.normal(jax.random.fold_in(_tk, 500 + 22), (1000, 128), jnp.float32)
        tbl_23 = 0.05 * jax.random.normal(jax.random.fold_in(_tk, 500 + 23), (1250, 128), jnp.float32)
        tbl_24 = 0.05 * jax.random.normal(jax.random.fold_in(_tk, 500 + 24), (1250, 128), jnp.float32)
        tbl_25 = 0.05 * jax.random.normal(jax.random.fold_in(_tk, 500 + 25), (1250, 128), jnp.float32)
        _rk = jax.random.fold_in(_tk, 7)
        r_dense_features = -0.000520686 + 1.00062 * jax.random.normal(jax.random.fold_in(_rk, 101), (512, 128), jnp.float32)
        W_top1 = 0.0405887 * jax.random.normal(jax.random.fold_in(_tk, 801), (607, 512), jnp.float32)
        W_top2 = 0.0441942 * jax.random.normal(jax.random.fold_in(_tk, 802), (512, 256), jnp.float32)
        W_top3 = 0.0625 * jax.random.normal(jax.random.fold_in(_tk, 803), (256, 1), jnp.float32)
        b_top1 = jnp.zeros((512,), jnp.float32)
        b_top2 = jnp.zeros((256,), jnp.float32)
        return (r_dense_features, ids, tbl_0, tbl_1, tbl_2, tbl_3, tbl_4, tbl_5, tbl_6, tbl_7, tbl_8, tbl_9, tbl_10, tbl_11, tbl_12, tbl_13, tbl_14, tbl_15, tbl_16, tbl_17, tbl_18, tbl_19, tbl_20, tbl_21, tbl_22, tbl_23, tbl_24, tbl_25, W_top1, b_top1, W_top2, b_top2, W_top3)
    r_dense_features, ids, tbl_0, tbl_1, tbl_2, tbl_3, tbl_4, tbl_5, tbl_6, tbl_7, tbl_8, tbl_9, tbl_10, tbl_11, tbl_12, tbl_13, tbl_14, tbl_15, tbl_16, tbl_17, tbl_18, tbl_19, tbl_20, tbl_21, tbl_22, tbl_23, tbl_24, tbl_25, W_top1, b_top1, W_top2, b_top2, W_top3 = _rec_inputs()

    def _L0_rec_setup():
        import jax, jax.numpy as jnp
        import numpy as np
        NUM_SPARSE = 26
        EMBED_DIM = 128
        BATCH = 2048
        key = jax.random.key(seed)
        k1, k2 = jax.random.split(key)
        dense_features = jax.random.normal(k1, (BATCH, EMBED_DIM), dtype=jnp.float32)
        sparse_features = jax.random.normal(k2, (BATCH, NUM_SPARSE, EMBED_DIM), dtype=jnp.float32)
        return {'dense_features': dense_features, 'sparse_features': sparse_features}
    _L0_rec_all = _L0_rec_setup()
    _L0_rec_in = {k: v for k, v in _L0_rec_all.items() if k in ()}
    del _L0_rec_all
    return {'r_dense_features': r_dense_features, 'ids': ids, 'tbl_0': tbl_0, 'tbl_1': tbl_1, 'tbl_2': tbl_2, 'tbl_3': tbl_3, 'tbl_4': tbl_4, 'tbl_5': tbl_5, 'tbl_6': tbl_6, 'tbl_7': tbl_7, 'tbl_8': tbl_8, 'tbl_9': tbl_9, 'tbl_10': tbl_10, 'tbl_11': tbl_11, 'tbl_12': tbl_12, 'tbl_13': tbl_13, 'tbl_14': tbl_14, 'tbl_15': tbl_15, 'tbl_16': tbl_16, 'tbl_17': tbl_17, 'tbl_18': tbl_18, 'tbl_19': tbl_19, 'tbl_20': tbl_20, 'tbl_21': tbl_21, 'tbl_22': tbl_22, 'tbl_23': tbl_23, 'tbl_24': tbl_24, 'tbl_25': tbl_25, 'W_top1': W_top1, 'b_top1': b_top1, 'W_top2': W_top2, 'b_top2': b_top2, 'W_top3': W_top3}

def reference(r_dense_features, ids, tbl_0, tbl_1, tbl_2, tbl_3, tbl_4, tbl_5, tbl_6, tbl_7, tbl_8, tbl_9, tbl_10, tbl_11, tbl_12, tbl_13, tbl_14, tbl_15, tbl_16, tbl_17, tbl_18, tbl_19, tbl_20, tbl_21, tbl_22, tbl_23, tbl_24, tbl_25, W_top1, b_top1, W_top2, b_top2, W_top3):
    import jax
    import jax.numpy as jnp

    def _L0_rec_ref(dense_features, sparse_features):
        import jax, jax.numpy as jnp
        import numpy as np
        NUM_SPARSE = 26
        EMBED_DIM = 128
        BATCH = 2048
        F = NUM_SPARSE + 1
        combined = jnp.concatenate([dense_features[:, None, :], sparse_features], axis=1)
        interactions = jnp.einsum('bfd,bgd->bfg', combined, combined)
        iu, ju = jnp.triu_indices(F, k=1)
        interactions_flat = interactions[:, iu, ju]
        return jnp.concatenate([dense_features, interactions_flat], axis=1)
    e = jnp.stack([tbl_0[ids[:, 0]], tbl_1[ids[:, 1]], tbl_2[ids[:, 2]], tbl_3[ids[:, 3]], tbl_4[ids[:, 4]], tbl_5[ids[:, 5]], tbl_6[ids[:, 6]], tbl_7[ids[:, 7]], tbl_8[ids[:, 8]], tbl_9[ids[:, 9]], tbl_10[ids[:, 10]], tbl_11[ids[:, 11]], tbl_12[ids[:, 12]], tbl_13[ids[:, 13]], tbl_14[ids[:, 14]], tbl_15[ids[:, 15]], tbl_16[ids[:, 16]], tbl_17[ids[:, 17]], tbl_18[ids[:, 18]], tbl_19[ids[:, 19]], tbl_20[ids[:, 20]], tbl_21[ids[:, 21]], tbl_22[ids[:, 22]], tbl_23[ids[:, 23]], tbl_24[ids[:, 24]], tbl_25[ids[:, 25]]], axis=1)
    z = _L0_rec_ref(r_dense_features, e)
    z = z.reshape(z.shape[0], -1)
    h = jnp.concatenate([z, r_dense_features], axis=1)
    h = jnp.maximum(h @ W_top1 + b_top1, 0.0)
    h = jnp.maximum(h @ W_top2 + b_top2, 0.0)
    y = h @ W_top3
    return y

_drawn_inputs = setup_inputs


def setup_inputs(seed=0):
    import zlib

    import numpy as np

    out = dict(_drawn_inputs(seed))
    spreads = {'b_top1': (0.0, 0.1), 'b_top2': (0.0, 0.1)}
    factors = {}
    for name, (base, spread) in spreads.items():
        noise = np.random.default_rng([zlib.crc32(name.encode()), seed]).standard_normal(out[name].shape)
        drawn = base * np.exp(spread * noise) if base else spread * noise
        out[name] = jnp.asarray(drawn.astype(out[name].dtype))
    for name, factor in factors.items():
        out[name] = (out[name] * factor).astype(out[name].dtype)
    return out
```

```python
import numpy as np
import concourse.bass as bass
from concourse import mybir
from contextlib import ExitStack


TABLES = 26
FEATS = TABLES + 1
DIM = 128
BATCH = 512
ROWS = 128
TILES = BATCH // ROWS
H1, H2 = 512, 256
PAIRS = FEATS * (FEATS - 1) // 2
SHIFTS = FEATS // 2
CHUNKS = 3
CHUNK_F = FEATS // CHUNKS
CHUNK = CHUNK_F * SHIFTS


def pair_rows():
    iu, ju = np.triu_indices(FEATS, k=1)
    row = {(int(a), int(b)): n for n, (a, b) in enumerate(zip(iu, ju))}
    return [row[min(f, (f + k) % FEATS), max(f, (f + k) % FEATS)]
            for f in range(FEATS) for k in range(1, SHIFTS + 1)]


def build(nc, dense, ids, tables, w_dense, w_pairs, b1, w2, b2, w3, out):
    fp32 = mybir.dt.float32
    i32 = mybir.dt.int32
    ALU = mybir.AluOpType
    ACT = mybir.ActivationFunctionType

    Q = 32
    QUADS = ROWS // Q
    GROUP = 4
    GROUPS = [list(range(g, min(g + GROUP, FEATS))) for g in range(0, FEATS, GROUP)]
    NG = len(GROUPS)
    NG_DVE = (NG + 1) // 2
    NG_ACT = NG // 2
    K1 = H1 // 128
    WRAPPED = FEATS + SHIFTS

    ctx = ExitStack()
    with ctx:
        def sb(name, shape, dt=fp32):
            return ctx.enter_context(nc.sbuf_tensor(name, shape, dt))

        def ps(name, shape, dt=fp32):
            return ctx.enter_context(nc.psum_tensor(name, shape, dt))

        def sem(name):
            return ctx.enter_context(nc.semaphore(name))

        identity = sb("identity", [128, 128])
        ids_all = sb("ids_all", [ROWS, TILES * TABLES], i32)
        ids_now = sb("ids_now", [ROWS, 2, TABLES], i32)
        w_dense_2 = sb("w_dense_2", [DIM, 2, H1])
        w_dense_sum = sb("w_dense_sum", [DIM, H1])
        w_pairs_sb = sb("w_pairs_sb", [CHUNK + 1, CHUNKS, H1])
        w2_sb = sb("w2_sb", [128, K1, H2])
        b2_sb = sb("b2_sb", [ROWS, H2])
        w3_sb = sb("w3_sb", [ROWS, H2])
        rows = sb("rows", [ROWS, FEATS, DIM])
        cols = sb("cols", [DIM, FEATS, ROWS])
        inter = sb("inter", [ROWS, WRAPPED * 32])
        packed = sb("packed", [ROWS, PAIRS])
        pairs = sb("pairs", [CHUNK + 1, CHUNKS, ROWS])
        h1 = sb("h1", [ROWS, H1])
        h1_cols = sb("h1_cols", [128, K1, ROWS])
        h2 = sb("h2", [ROWS, H2])
        h2_w3 = sb("h2_w3", [ROWS, H2])
        y = sb("y", [ROWS, 1])

        ps_cols = [ps(f"ps_cols{i}", [DIM, GROUP, ROWS]) for i in range(2)]
        ps_gram = ps("ps_gram", [128, 2, 512])
        ps_pairs = ps("ps_pairs", [128, CHUNKS, ROWS])
        ps_h1 = ps("ps_h1", [ROWS, H1])
        ps_h1_cols = ps("ps_h1_cols", [128, K1, ROWS])
        ps_h2 = ps("ps_h2", [ROWS, H2])

        ids_loaded = sem("ids_loaded")
        ids_copied = sem("ids_copied")
        weights_loaded = sem("weights_loaded")
        dense_loaded = sem("dense_loaded")
        group_gathered = [sem(f"group_gathered{g}") for g in range(NG)]
        groups_begun = sem("groups_begun")
        identity_zeroed = sem("identity_zeroed")
        identity_ready = sem("identity_ready")
        ones_ready = sem("ones_ready")
        gram_pads_ready = sem("gram_pads_ready")
        w_dense_ready = sem("w_dense_ready")
        group_transposed = sem("group_transposed")
        cols_ready_dve = sem("cols_ready_dve")
        cols_ready_act = sem("cols_ready_act")
        gram_ready = sem("gram_ready")
        inter_ready = sem("inter_ready")
        packed_ready = sem("packed_ready")
        pairs_transposed = sem("pairs_transposed")
        pairs_ready = sem("pairs_ready")
        h1_summed = sem("h1_summed")
        h1_ready = sem("h1_ready")
        h1_transposed = sem("h1_transposed")
        h1_cols_ready = sem("h1_cols_ready")
        h2_summed = sem("h2_summed")
        h2_biased = sem("h2_biased")
        y_ready = sem("y_ready")
        out_stored = sem("out_stored")

        inter_at = inter[:, 0:1]

        inter_pairs = bass.AP(inter_at.tensor, inter_at.offset + 32,
                              [list(inter_at.ap[0]), [33, FEATS], [32, SHIFTS]])

        block = ctx.enter_context(nc.Block())

        @block.sync
        def _(sp):
            sp.dma_start(ids_all[:, :].rearrange("p (t f) -> p t f", t=TILES),
                         ids.rearrange("(t p) f -> p t f", p=ROWS)).then_inc(ids_loaded, 16)
            sp.dma_start(rows[:, 0, :], dense[0:ROWS, :]).then_inc(dense_loaded, 16)
            sp.dma_start(w_dense_2[:, :, :], w_dense.rearrange("(a p) n -> p a n", a=2)).then_inc(weights_loaded, 16)
            sp.dma_start(w_pairs_sb[0:CHUNK, :, :],
                         w_pairs.rearrange("(c p) n -> p c n", c=CHUNKS)).then_inc(weights_loaded, 16)
            sp.dma_start(w_pairs_sb[CHUNK:CHUNK + 1, CHUNKS - 1, :],
                         b1.rearrange("(a n) -> a n", a=1)).then_inc(weights_loaded, 16)
            sp.dma_start(w2_sb[:, :, :], w2.rearrange("(c p) n -> p c n", c=K1)).then_inc(weights_loaded, 16)
            sp.dma_start(b2_sb[:, :], b2.rearrange("(a n) -> a n", a=1).to_broadcast([ROWS, H2]))\
              .then_inc(weights_loaded, 16)
            sp.dma_start(w3_sb[:, :], w3.rearrange("n a -> a n").to_broadcast([ROWS, H2]))\
              .then_inc(weights_loaded, 16)
            with sp.Fori(0, TILES - 1) as t:
                sp.wait_ge(group_transposed, NG * (t + 1) + 1)
                sp.dma_start(rows[:, 0, :], dense[bass.ds((t + 1) * ROWS, ROWS), :]).then_inc(dense_loaded, 16)
                sp.wait_ge(y_ready, t + 1)
                sp.dma_start(out[bass.ds(t * ROWS, ROWS), :], y[:, :]).then_inc(out_stored, 16)
            sp.wait_ge(y_ready, TILES)
            sp.dma_start(out[(TILES - 1) * ROWS:, :], y[:, :]).then_inc(out_stored, 16)
            sp.wait_ge(out_stored, 16 * TILES)

        @block.gpsimd
        def _(pool):
            nc.gpsimd.memset(identity[:, :], 0.0).then_inc(identity_zeroed, 1)
            pool.wait_ge(identity_zeroed, 1)
            nc.gpsimd.affine_select(out=identity[:, :], in_=identity[:, :], compare_op=ALU.not_equal, fill=1.0,
                                    base=0, pattern=[[-1, 128]], channel_multiplier=1).then_inc(identity_ready, 1)
            pool.wait_ge(ids_loaded, 16)
            with pool.Fori(0, TILES // 2) as turn:
                for half in range(2):
                    t = turn * 2 + half
                    pool.wait_ge(group_transposed, NG * t)
                    pool.sem_inc(groups_begun, 1)
                    nc.gpsimd.tensor_copy(ids_now[:, half, :], ids_all[:, bass.ds(t * TABLES, TABLES)])\
                      .then_inc(ids_copied, 1)
                    pool.wait_ge(ids_copied, t + 1)
                    pool.sem_inc(groups_begun, 1)
                    for g, feats in enumerate(GROUPS):
                        pool.wait_ge(group_transposed, NG * t + g + 1)
                        pool.sem_inc(groups_begun, 1)
                        for f in feats:
                            if f == 0:
                                continue
                            nc.gpsimd.indirect_dma_start(
                                out=rows[:, f, :], out_offset=None, in_=tables[f - 1][:, :],
                                in_offset=bass.IndirectOffsetOnAxis(ap=ids_now[:, half, f - 1:f], axis=0),
                            ).then_inc(group_gathered[g], 16)

        @block.tensor
        def _(pe):
            pe.wait_ge(identity_ready, 1)
            pe.sem_inc(group_transposed, NG)
            with pe.Fori(0, TILES) as t:
                for g, feats in enumerate(GROUPS):
                    if g == 0:
                        pe.wait_ge(dense_loaded, 16 * (t + 1))
                        pe.wait_ge(group_gathered[g], 16 * (len(feats) - 1) * (t + 1))
                    else:
                        pe.wait_ge(group_gathered[g], 16 * len(feats) * (t + 1))
                    if g % 2 == 0:
                        pe.wait_ge(cols_ready_dve, NG_DVE * t + g // 2)
                    else:
                        pe.wait_ge(cols_ready_act, NG_ACT * t + g // 2)
                    for i, f in enumerate(feats):
                        last = nc.tensor.transpose(ps_cols[g % 2][:, i, :], rows[:, f, :], identity[:, :])
                    last.then_inc(group_transposed, 1)
                pe.wait_ge(cols_ready_dve, NG_DVE * (t + 1))
                pe.wait_ge(cols_ready_act, NG_ACT * (t + 1))
                pe.wait_ge(gram_pads_ready, 1)
                pe.wait_ge(inter_ready, 2 * t)
                for q in range(Q):
                    at = q % (Q // 2) * FEATS
                    for j in range(QUADS):
                        p = Q * j + q
                        last = nc.tensor.matmul(ps_gram[32 * j:32 * j + FEATS, q // (Q // 2), at:at + FEATS],
                                                cols[:, :, p], cols[:, :, p], start=True, stop=True,
                                                tile_position=(0, 32 * j))
                last.then_inc(gram_ready, 1)
                pe.wait_ge(packed_ready, t + 1)
                for c in range(CHUNKS):
                    last = nc.tensor.transpose(ps_pairs[0:CHUNK, c, :], packed[:, CHUNK * c:CHUNK * (c + 1)], identity[:, :])
                last.then_inc(pairs_transposed, 1)
                pe.wait_ge(w_dense_ready, 1)
                nc.tensor.matmul(ps_h1[:, :], cols[:, 0, :], w_dense_sum[:, :], start=True, stop=False)
                pe.wait_ge(pairs_ready, t + 1)
                for c in range(CHUNKS):
                    k = CHUNK + (c == CHUNKS - 1)
                    last = nc.tensor.matmul(ps_h1[:, :], pairs[0:k, c, :], w_pairs_sb[0:k, c, :],
                                            start=False, stop=c == CHUNKS - 1)
                last.then_inc(h1_summed, 1)
                pe.wait_ge(h1_ready, t + 1)
                for c in range(K1):
                    last = nc.tensor.transpose(ps_h1_cols[:, c, :], h1[:, 128 * c:128 * (c + 1)], identity[:, :])
                last.then_inc(h1_transposed, 1)
                pe.wait_ge(h1_cols_ready, t + 1)
                pe.wait_ge(h2_biased, t)
                for c in range(K1):
                    last = nc.tensor.matmul(ps_h2[:, :], h1_cols[:, c, :], w2_sb[:, c, :],
                                            start=c == 0, stop=c == K1 - 1)
                last.then_inc(h2_summed, 1)

        @block.scalar
        def _(act):
            with act.Fori(0, TILES) as t:
                for n in range(NG_ACT):
                    g = 2 * n + 1
                    act.wait_ge(group_transposed, NG * (t + 1) + g + 1)
                    nc.scalar.activation(cols[:, GROUPS[g][0]:GROUPS[g][-1] + 1, :],
                                         ps_cols[1][:, 0:len(GROUPS[g]), :], ACT.Copy).then_inc(cols_ready_act, 1)
                act.wait_ge(inter_ready, 2 * (t + 1))
                nc.scalar.activation(packed[:, :].rearrange("p (f k) -> p f k", k=SHIFTS), inter_pairs, ACT.Copy)\
                  .then_inc(packed_ready, 1)
                act.wait_ge(pairs_transposed, t + 1)
                act.wait_ge(ones_ready, 1)
                nc.scalar.activation(pairs[0:CHUNK, :, :], ps_pairs[0:CHUNK, :, :], ACT.Copy).then_inc(pairs_ready, 1)
                act.wait_ge(h1_summed, t + 1)
                nc.scalar.activation(h1[:, :], ps_h1[:, :], ACT.Relu).then_inc(h1_ready, 1)
                act.wait_ge(h1_transposed, t + 1)
                nc.scalar.activation(h1_cols[:, :, :], ps_h1_cols[:, :, :], ACT.Copy).then_inc(h1_cols_ready, 1)

        @block.vector
        def _(dve):
            nc.vector.memset(ps_gram[:, :, :], 0.0).then_inc(gram_pads_ready, 1)
            nc.vector.memset(pairs[:, :, :], 1.0).then_inc(ones_ready, 1)
            dve.wait_ge(weights_loaded, 6 * 16)
            nc.vector.tensor_tensor(w_dense_sum[:, :], w_dense_2[:, 0, :], w_dense_2[:, 1, :], ALU.add)\
              .then_inc(w_dense_ready, 1)
            with dve.Fori(0, TILES) as t:
                for n in range(NG_DVE):
                    g = 2 * n
                    dve.wait_ge(group_transposed, NG * (t + 1) + g + 1)
                    nc.vector.tensor_copy(cols[:, GROUPS[g][0]:GROUPS[g][-1] + 1, :],
                                          ps_cols[0][:, 0:len(GROUPS[g]), :]).then_inc(cols_ready_dve, 1)
                dve.wait_ge(gram_ready, t + 1)
                gram = ps_gram[:, :, 0:Q // 2 * FEATS].rearrange("p h (q m) -> p m h q", m=FEATS)
                for m0, m1, at in ((0, FEATS, 0), (0, SHIFTS, FEATS)):
                    nc.vector.transpose(inter[:, 32 * at:32 * (at + m1 - m0)].rearrange("p (m h f) -> p m h f", h=2, f=Q // 2),
                                        gram[:, m0:m1, :, :]).then_inc(inter_ready, 1)
                dve.wait_ge(h2_summed, t + 1)
                nc.vector.tensor_tensor(h2[:, :], ps_h2[:, :], b2_sb[:, :], ALU.add).then_inc(h2_biased, 1)
                dve.wait_ge(h2_biased, t + 1)
                dve.wait_ge(out_stored, 16 * t)
                nc.vector.scalar_tensor_tensor(out=h2_w3[:, :], in0=h2[:, :], scalar=0.0, in1=w3_sb[:, :],
                                               op0=ALU.max, op1=ALU.mult, accum_out=y[:, :]).then_inc(y_ready, 1)


def kernel(**inputs):
    import concourse.bacc as bacc
    from concourse.bass_utils import run_bass_kernel_spmd

    nc = bacc.Bacc("TRN2", target_bir_lowering=False, num_devices=1)
    w1 = np.asarray(inputs["W_top1"])
    laid_out = {
        "dense": inputs["r_dense_features"], "ids": inputs["ids"],
        **{f"tbl_{n}": inputs[f"tbl_{n}"] for n in range(TABLES)},
        "w_dense": np.concatenate([w1[:DIM], w1[DIM + PAIRS:]], axis=0),
        "w_pairs": w1[DIM:DIM + PAIRS][pair_rows()],
        "b1": inputs["b_top1"], "w2": inputs["W_top2"], "b2": inputs["b_top2"], "w3": inputs["W_top3"],
    }
    arrays, aps = {}, {}
    for name, a in laid_out.items():
        a = np.ascontiguousarray(a)
        arrays[f"in_{name}"] = a
        aps[name] = nc.dram_tensor(f"in_{name}", a.shape, mybir.dt.from_np(a.dtype), kind="ExternalInput").ap()
    out = nc.dram_tensor("out_y", (BATCH, 1), mybir.dt.float32, kind="ExternalOutput").ap()
    build(nc, aps["dense"], aps["ids"], [aps[f"tbl_{n}"] for n in range(TABLES)], aps["w_dense"], aps["w_pairs"],
          aps["b1"], aps["w2"], aps["b2"], aps["w3"], out)
    r = run_bass_kernel_spmd(nc, [arrays], core_ids=[0])
    return r.results[0]["out_y"]
```

```python
import numpy as np
import concourse.bass as bass
from concourse import mybir
from contextlib import ExitStack


TABLE_ROWS = [1250, 12500, 12500, 1000, 1250, 1250, 1250, 1250, 125000, 12500, 1250, 1250, 12500, 1250, 12500,
              1000, 1000, 12500, 12500, 1000, 12500, 1250, 1000, 1250, 1250, 1250]
TABLES = len(TABLE_ROWS)
FEATS = TABLES + 1
DIM = 128
BATCH = 512
ROWS = 128
TILES = BATCH // ROWS
H1, H2 = 512, 256
PAIRS = FEATS * (FEATS - 1) // 2

LOOKED_UP = [3, 15, 16, 19, 22, 0, 4]
GATHERED = [n for n in range(TABLES) if n not in LOOKED_UP]
NL, NGA = len(LOOKED_UP), len(GATHERED)
ORDER = [n + 1 for n in LOOKED_UP] + [0] + [n + 1 for n in GATHERED]
DENSE = NL

SHIFTS = FEATS // 2
CHUNKS = 3
CHUNK_F = FEATS // CHUNKS
CHUNK = CHUNK_F * SHIFTS

LP = 125
LP_MAIN = 120


def pair_rows():
    iu, ju = np.triu_indices(FEATS, k=1)
    row = {(int(a), int(b)): n for n, (a, b) in enumerate(zip(iu, ju))}
    rows = []
    for f in range(FEATS):
        for k in range(1, SHIFTS + 1):
            a, b = ORDER[f], ORDER[(f + k) % FEATS]
            rows.append(row[min(a, b), max(a, b)])
    return rows


def build(nc, dense, ids_gather, ids_lookup, tables, w_dense, w_pairs, b1, w2, b2, w3, out):
    fp32 = mybir.dt.float32
    fp32r = mybir.dt.float32r
    i32 = mybir.dt.int32
    ALU = mybir.AluOpType
    ACT = mybir.ActivationFunctionType

    Q = 32
    QUADS = ROWS // Q
    FIRST = DENSE
    GROUP = 4
    GROUPS = [list(range(g, min(g + GROUP, FEATS - 1))) for g in range(FIRST, FEATS - 1, GROUP)] + [[FEATS - 1]]
    NG = len(GROUPS)
    NG_DVE = (NG + 1) // 2
    NG_ACT = NG // 2
    LAG = 1
    AHEAD = 2
    WHERE = {g: min(g - AHEAD + 1, 4) for g in range(AHEAD, NG)}
    K1 = H1 // 128
    HALVES = 2
    HALF = H1 // HALVES
    KH = K1 // HALVES
    WRAPPED = FEATS + SHIFTS
    COUNTS = [TABLE_ROWS[n] // LP for n in LOOKED_UP]
    CMAX = max(COUNTS)
    assert all(c * LP == TABLE_ROWS[n] for c, n in zip(COUNTS, LOOKED_UP))

    ctx = ExitStack()
    with ctx:
        def sb(name, shape, dt=fp32):
            return ctx.enter_context(nc.sbuf_tensor(name, shape, dt))

        def ps(name, shape, dt=fp32):
            return ctx.enter_context(nc.psum_tensor(name, shape, dt))

        def sem(name):
            return ctx.enter_context(nc.semaphore(name))

        identity = sb("identity", [128, 128])
        row_of = {c: sb(f"row_of{c}", [LP, c]) for c in sorted(set(COUNTS))}
        ids_all = sb("ids_all", [ROWS, TILES * NGA], i32)
        ids_now = sb("ids_now", [ROWS, 2, NGA], i32)
        w_dense_2 = sb("w_dense_2", [DIM, 2, H1])
        w_dense_sum = sb("w_dense_sum", [DIM, H1])
        w_pairs_sb = sb("w_pairs_sb", [CHUNK + 1, CHUNKS, H1])
        w2_sb = sb("w2_sb", [128, K1, H2])
        b2_sb = sb("b2_sb", [ROWS, H2])
        w3_sb = sb("w3_sb", [ROWS, H2])
        ids_wide = sb("ids_wide", [LP, NL, BATCH], i32)
        table = [sb(f"table{i}", [LP, COUNTS[i], DIM]) for i in range(NL)]
        table_high = [sb(f"table_high{i}", [LP, CMAX, DIM], fp32r) for i in range(2)]
        table_low = [sb(f"table_low{i}", [LP, CMAX, DIM], fp32r) for i in range(2)]
        one_hot = [sb(f"one_hot{i}", [LP, CMAX, BATCH], fp32r) for i in range(2)]
        looked_up = sb("looked_up", [DIM, NL, BATCH])
        rows = sb("rows", [ROWS, FEATS - FIRST, DIM])
        cols = sb("cols", [DIM, FEATS, ROWS])
        inter = sb("inter", [ROWS, WRAPPED * 32])
        packed = sb("packed", [ROWS, PAIRS])
        pairs = sb("pairs", [CHUNK + 1, CHUNKS, ROWS])
        h1 = sb("h1", [ROWS, H1])
        h1_cols = sb("h1_cols", [128, K1, ROWS])
        h2 = sb("h2", [ROWS, H2])
        h2_w3 = sb("h2_w3", [ROWS, H2])
        y = sb("y", [ROWS, 1])

        ps_cols = [ps(f"ps_cols{i}", [DIM, GROUP, ROWS]) for i in range(2)]
        ps_gram = ps("ps_gram", [128, 2, 512])
        bank = [ps(f"bank{i}", [128, 512]) for i in range(4)]
        ps_lookup = bank[0:2]
        ps_h1 = [bank[0][:, 0:HALF], bank[1][:, 0:HALF]]
        ps_pairs = [bank[3][0:CHUNK, 0:ROWS], bank[2][0:CHUNK, 0:ROWS], ps_gram[0:CHUNK, 1, 0:ROWS]]
        ps_h1_cols = [x.rearrange("p (c n) -> p c n", c=KH) for x in
                      (ps_gram[:, 0, 0:KH * ROWS], bank[3][:, 0:KH * ROWS])]
        ps_h2 = bank[2][:, 0:H2]

        ids_loaded = sem("ids_loaded")
        ids_copied = sem("ids_copied")
        table_loaded = [sem(f"table_loaded{i}") for i in range(NL)]
        weights_loaded = sem("weights_loaded")
        dense_loaded = sem("dense_loaded")
        group_gathered = [sem(f"group_gathered{g}") for g in range(NG)]
        groups_begun = sem("groups_begun")
        identity_zeroed = sem("identity_zeroed")
        identity_ready = sem("identity_ready")
        row_of_ready = sem("row_of_ready")
        ones_ready = sem("ones_ready")
        gram_pads_ready = sem("gram_pads_ready")
        w_dense_ready = sem("w_dense_ready")
        high_ready = sem("high_ready")
        low_ready = sem("low_ready")
        one_hot_ready = sem("one_hot_ready")
        lookup_summed = sem("lookup_summed")
        lookup_copied = sem("lookup_copied")
        group_transposed = sem("group_transposed")
        cols_ready_dve = sem("cols_ready_dve")
        cols_ready_act = sem("cols_ready_act")
        looked_up_in_cols = sem("looked_up_in_cols")
        dense_multiplied = sem("dense_multiplied")
        gram_ready = sem("gram_ready")
        inter_ready = sem("inter_ready")
        packed_ready = sem("packed_ready")
        pairs_transposed = sem("pairs_transposed")
        pairs_ready = sem("pairs_ready")
        h1_summed = sem("h1_summed")
        h1_ready = sem("h1_ready")
        h1_transposed = sem("h1_transposed")
        h1_cols_ready = sem("h1_cols_ready")
        h2_summed = sem("h2_summed")
        h2_biased = sem("h2_biased")
        y_ready = sem("y_ready")
        y_free = sem("y_free")
        out_stored = sem("out_stored")

        inter_at = inter[:, 0:1]

        def inter_pairs(c):
            return bass.AP(inter_at.tensor, inter_at.offset + 32 + 33 * CHUNK_F * c,
                           [list(inter_at.ap[0]), [33, CHUNK_F], [32, SHIFTS]])

        block = ctx.enter_context(nc.Block())

        @block.sync
        def _(sp):
            sp.dma_start(ids_all[:, :], ids_gather).then_inc(ids_loaded, 16)
            for i in range(NL):
                c = COUNTS[i]
                sp.dma_start(ids_wide[:, i, :], ids_lookup[i:i + 1, :].to_broadcast([LP, BATCH]))\
                  .then_inc(table_loaded[i], 16)
                sp.dma_start(table[i][0:LP_MAIN, :, :],
                             tables[LOOKED_UP[i]][0:c * LP_MAIN, :].rearrange("(p c) d -> p c d", c=c))\
                  .then_inc(table_loaded[i], 16)
                sp.dma_start(table[i][LP_MAIN:LP, :, :],
                             tables[LOOKED_UP[i]][c * LP_MAIN:, :].rearrange("(p c) d -> p c d", c=c))\
                  .then_inc(table_loaded[i], 16)
                if i == 0:
                    sp.dma_start(rows[:, 0, :], dense[0:ROWS, :]).then_inc(dense_loaded, 16)
            sp.dma_start(w_dense_2[:, :, :], w_dense.rearrange("(a p) n -> p a n", a=2)).then_inc(weights_loaded, 16)
            sp.dma_start(w_pairs_sb[0:CHUNK, :, :],
                         w_pairs.rearrange("(c p) n -> p c n", c=CHUNKS)).then_inc(weights_loaded, 16)
            sp.dma_start(w_pairs_sb[CHUNK:CHUNK + 1, CHUNKS - 1, :],
                         b1.rearrange("(a n) -> a n", a=1)).then_inc(weights_loaded, 16)
            sp.dma_start(w2_sb[:, :, :], w2.rearrange("(c p) n -> p c n", c=K1)).then_inc(weights_loaded, 16)
            sp.dma_start(b2_sb[:, :], b2.rearrange("(a n) -> a n", a=1).to_broadcast([ROWS, H2]))\
              .then_inc(weights_loaded, 16)
            sp.dma_start(w3_sb[:, :], w3.rearrange("n a -> a n").to_broadcast([ROWS, H2]))\
              .then_inc(weights_loaded, 16)
            sp.sem_inc(y_free, 1)
            sp.wait_ge(group_transposed, NG + 1)
            sp.dma_start(rows[:, 0, :], dense[ROWS:2 * ROWS, :]).then_inc(dense_loaded, 16)
            with sp.Fori(0, TILES - 2) as t:
                sp.wait_ge(group_transposed, NG * (t + 2) + 1)
                sp.dma_start(rows[:, 0, :], dense[bass.ds((t + 2) * ROWS, ROWS), :]).then_inc(dense_loaded, 16)
                sp.wait_ge(y_ready, t + 1)
                sp.dma_start(out[bass.ds(t * ROWS, ROWS), :], y[:, :]).then_inc(out_stored, 16)
                sp.wait_ge(out_stored, 16 * (t + 1))
                sp.sem_inc(y_free, 1)
            for t in (TILES - 2, TILES - 1):
                sp.wait_ge(y_ready, t + 1)
                sp.dma_start(out[t * ROWS:(t + 1) * ROWS, :], y[:, :]).then_inc(out_stored, 16)
                sp.wait_ge(out_stored, 16 * (t + 1))
                sp.sem_inc(y_free, 1)

        @block.gpsimd
        def _(pool):
            nc.gpsimd.memset(identity[:, :], 0.0).then_inc(identity_zeroed, 1)
            pool.wait_ge(identity_zeroed, 1)
            nc.gpsimd.affine_select(out=identity[:, :], in_=identity[:, :], compare_op=ALU.not_equal, fill=1.0,
                                    base=0, pattern=[[-1, 128]], channel_multiplier=1).then_inc(identity_ready, 1)
            for c, t in row_of.items():
                nc.gpsimd.iota(t[:, :], pattern=[[1, c]], base=0, channel_multiplier=c,
                               allow_small_or_imprecise_dtypes=True).then_inc(row_of_ready, 1)
            pool.wait_ge(ids_loaded, 16)
            with pool.Fori(0, TILES // 2) as turn:
                for half in range(2):
                    t = turn * 2 + half
                    nc.gpsimd.tensor_copy(ids_now[:, half, :], ids_all[:, bass.ds(t * NGA, NGA)])\
                      .then_inc(ids_copied, 1)
                    pool.wait_ge(ids_copied, t + 1)
                    pool.sem_inc(groups_begun, 1)
                    for g, feats in enumerate(GROUPS):
                        pool.wait_ge(group_transposed, NG * t + g + 1)
                        pool.sem_inc(groups_begun, 1)
                        for f in feats:
                            if f == DENSE:
                                continue
                            n = f - DENSE - 1
                            nc.gpsimd.indirect_dma_start(
                                out=rows[:, f - FIRST, :], out_offset=None, in_=tables[GATHERED[n]][:, :],
                                in_offset=bass.IndirectOffsetOnAxis(ap=ids_now[:, half, n:n + 1], axis=0),
                            ).then_inc(group_gathered[g], 16)

        @block.tensor
        def _(pe):
            def look_up(i):
                pe.wait_ge(high_ready, i + 1)
                pe.wait_ge(low_ready, i + 1)
                if i >= 2:
                    pe.wait_ge(lookup_copied, i - 1)
                for c in range(COUNTS[i]):
                    pe.wait_ge(one_hot_ready, sum(COUNTS[:i]) + c + 1)
                    for part in (table_high, table_low):
                        last = nc.tensor.matmul(ps_lookup[i % 2][:, :], part[i % 2][:, c, :], one_hot[i % 2][:, c, :],
                                                start=c == 0 and part is table_high,
                                                stop=c == COUNTS[i] - 1 and part is table_low)
                last.then_inc(lookup_summed, 1)

            def transpose_group(g, t):
                feats = GROUPS[g]
                if g == 0:
                    pe.wait_ge(dense_loaded, 16 * (t + 1))
                    pe.wait_ge(group_gathered[g], 16 * (len(feats) - 1) * (t + 1))
                else:
                    pe.wait_ge(group_gathered[g], 16 * len(feats) * (t + 1))
                copied, to_tile = ((cols_ready_dve, NG_DVE), (cols_ready_act, NG_ACT))[g % 2]
                if g >= 2 or not isinstance(t, int):
                    pe.wait_ge(copied, to_tile * t + g // 2)
                for i, f in enumerate(feats):
                    last = nc.tensor.transpose(ps_cols[g % 2][:, i, :], rows[:, f - FIRST, :], identity[:, :])
                last.then_inc(group_transposed, 1)

            def gram(t):
                pe.wait_ge(cols_ready_dve, NG_DVE * (t + 1))
                pe.wait_ge(cols_ready_act, NG_ACT * (t + 1))
                pe.wait_ge(looked_up_in_cols, t + 1)
                for q in range(Q):
                    at = q % (Q // 2) * FEATS
                    for j in range(QUADS):
                        p = Q * j + q
                        last = nc.tensor.matmul(ps_gram[32 * j:32 * j + FEATS, q // (Q // 2), at:at + FEATS],
                                                cols[:, :, p], cols[:, :, p], start=True, stop=True,
                                                tile_position=(0, 32 * j))
                last.then_inc(gram_ready, 1)

            def layers(t, fill):
                for h in range(HALVES):
                    nc.tensor.matmul(ps_h1[h], cols[:, DENSE, :], w_dense_sum[:, h * HALF:(h + 1) * HALF],
                                     start=True, stop=False).then_inc(dense_multiplied, 1)
                for c in range(CHUNKS):
                    pe.wait_ge(packed_ready, CHUNKS * t + c + 1)
                    nc.tensor.transpose(ps_pairs[c], packed[:, CHUNK * c:CHUNK * (c + 1)],
                                        identity[:, :]).then_inc(pairs_transposed, 1)
                fill(1)
                for h in range(HALVES):
                    for c in range(CHUNKS):
                        if h == 0:
                            pe.wait_ge(pairs_ready, CHUNKS * t + c + 1)
                        k = CHUNK + (c == CHUNKS - 1)
                        last = nc.tensor.matmul(ps_h1[h], pairs[0:k, c, :],
                                                w_pairs_sb[0:k, c, h * HALF:(h + 1) * HALF],
                                                start=False, stop=c == CHUNKS - 1)
                    last.then_inc(h1_summed, 1)
                fill(2)
                for h in range(HALVES):
                    pe.wait_ge(h1_ready, HALVES * t + h + 1)
                    for c in range(h * KH, (h + 1) * KH):
                        last = nc.tensor.transpose(ps_h1_cols[h][:, c - h * KH, :], h1[:, 128 * c:128 * (c + 1)], identity[:, :])
                    last.then_inc(h1_transposed, 1)
                fill(3)
                for h in range(HALVES):
                    pe.wait_ge(h1_cols_ready, HALVES * t + h + 1)
                    for c in range(h * KH, (h + 1) * KH):
                        last = nc.tensor.matmul(ps_h2, h1_cols[:, c, :], w2_sb[:, c, :],
                                                start=c == 0, stop=c == K1 - 1)
                last.then_inc(h2_summed, 1)
                fill(4)

            pe.wait_ge(identity_ready, 1)
            pe.sem_inc(group_transposed, NG)
            for n in range(max(NG + LAG, NL)):
                if n < NL:
                    look_up(n)
                if 0 <= n - LAG < NG:
                    transpose_group(n - LAG, 0)
            pe.wait_ge(gram_pads_ready, 1)
            pe.wait_ge(w_dense_ready, 1)
            pe.wait_ge(lookup_copied, NL)
            with pe.Fori(0, TILES - 1) as t:
                for g in range(AHEAD):
                    transpose_group(g, t + 1)
                gram(t)
                layers(t, lambda n: [transpose_group(g, t + 1) for g in WHERE if WHERE[g] == n])
            gram(TILES - 1)
            layers(TILES - 1, lambda n: None)

        @block.scalar
        def _(act):
            def copy_group(g, t):
                act.wait_ge(group_transposed, NG * (t + 1) + g + 1)
                nc.scalar.activation(cols[:, GROUPS[g][0]:GROUPS[g][-1] + 1, :],
                                     ps_cols[1][:, 0:len(GROUPS[g]), :], ACT.Copy).then_inc(cols_ready_act, 1)

            def copy_lookup(i):
                act.wait_ge(lookup_summed, i + 1)
                nc.scalar.activation(looked_up[:, i, :], ps_lookup[i % 2][:, :], ACT.Copy).then_inc(lookup_copied, 1)

            def place_looked_up(t):
                at = t * ROWS
                src = looked_up[:, :, bass.ds(at, ROWS)] if not isinstance(t, int) else looked_up[:, :, at:at + ROWS]
                nc.scalar.activation(cols[:, 0:NL, :], src, ACT.Copy).then_inc(looked_up_in_cols, 1)

            def layers(t, fill):
                for c in range(CHUNKS):
                    act.wait_ge(inter_ready, 2 * t + (1 if c == 0 else 2))
                    nc.scalar.activation(packed[:, CHUNK * c:CHUNK * (c + 1)].rearrange("p (f k) -> p f k", k=SHIFTS),
                                         inter_pairs(c), ACT.Copy).then_inc(packed_ready, 1)
                for c in range(CHUNKS):
                    act.wait_ge(pairs_transposed, CHUNKS * t + c + 1)
                    nc.scalar.activation(pairs[0:CHUNK, c, :], ps_pairs[c], ACT.Copy)\
                      .then_inc(pairs_ready, 1)
                fill(1)
                for h in range(HALVES):
                    act.wait_ge(h1_summed, HALVES * t + h + 1)
                    nc.scalar.activation(h1[:, h * HALF:(h + 1) * HALF], ps_h1[h], ACT.Relu).then_inc(h1_ready, 1)
                fill(2)
                for h in range(HALVES):
                    act.wait_ge(h1_transposed, HALVES * t + h + 1)
                    nc.scalar.activation(h1_cols[:, h * KH:(h + 1) * KH, :], ps_h1_cols[h], ACT.Copy).then_inc(h1_cols_ready, 1)
                fill(3)
                fill(4)

            for n in range(max(NG + LAG, NL) + 2):
                if n < NL:
                    act.wait_ge(table_loaded[n], 48)
                    if n >= 2:
                        act.wait_ge(lookup_summed, n - 1)
                    nc.scalar.activation(table_high[n % 2][:, 0:COUNTS[n], :], table[n][:, :, :], ACT.Copy)\
                      .then_inc(high_ready, 1)
                if 0 <= n - 2 < NL:
                    copy_lookup(n - 2)
                g = n - 2 - LAG
                if 0 <= g < NG and g % 2 == 1:
                    copy_group(g, 0)
            act.wait_ge(lookup_copied, NL)
            place_looked_up(0)
            act.wait_ge(ones_ready, 1)
            with act.Fori(0, TILES - 1) as t:
                act.wait_ge(gram_ready, t + 1)
                place_looked_up(t + 1)
                copy_group(1, t + 1)
                layers(t, lambda n: [copy_group(g, t + 1) for g in WHERE if WHERE[g] == n and g % 2 == 1])
            layers(TILES - 1, lambda n: None)

        @block.vector
        def _(dve):
            def copy_group(g, t):
                dve.wait_ge(group_transposed, NG * (t + 1) + g + 1)
                nc.vector.tensor_copy(cols[:, GROUPS[g][0]:GROUPS[g][-1] + 1, :],
                                      ps_cols[0][:, 0:len(GROUPS[g]), :]).then_inc(cols_ready_dve, 1)

            def prepare_lookup(i):
                c = COUNTS[i]
                dve.wait_ge(table_loaded[i], 48)
                if i >= 2:
                    dve.wait_ge(lookup_summed, i - 1)
                for n in range(c):
                    nc.vector.tensor_scalar(one_hot[i % 2][:, n, :], ids_wide[:, i, :], row_of[c][:, n:n + 1], None,
                                            ALU.is_equal).then_inc(one_hot_ready, 1)
                    if n == 0:
                        dve.wait_ge(high_ready, i + 1)
                        nc.vector.tensor_tensor(table_low[i % 2][:, 0:c, :], table[i][:, :, :],
                                                table_high[i % 2][:, 0:c, :].bitcast(fp32), ALU.subtract)\
                          .then_inc(low_ready, 1)

            def to_pairs(t):
                dve.wait_ge(gram_ready, t + 1)
                grams = ps_gram[:, :, 0:Q // 2 * FEATS].rearrange("p h (q m) -> p m h q", m=FEATS)
                for m, at in ((FEATS, 0), (SHIFTS, FEATS)):
                    nc.vector.transpose(inter[:, 32 * at:32 * (at + m)].rearrange("p (m h f) -> p m h f", h=2, f=Q // 2),
                                        grams[:, 0:m, :, :]).then_inc(inter_ready, 1)

            def finish(t):
                dve.wait_ge(h2_summed, t + 1)
                nc.vector.tensor_tensor(h2[:, :], ps_h2, b2_sb[:, :], ALU.add).then_inc(h2_biased, 1)
                dve.wait_ge(h2_biased, t + 1)
                dve.wait_ge(y_free, t + 1)
                nc.vector.scalar_tensor_tensor(out=h2_w3[:, :], in0=h2[:, :], scalar=0.0, in1=w3_sb[:, :],
                                               op0=ALU.max, op1=ALU.mult, accum_out=y[:, :]).then_inc(y_ready, 1)

            nc.vector.memset(ps_gram[:, :, :], 0.0).then_inc(gram_pads_ready, 1)
            nc.vector.memset(pairs[:, :, :], 1.0).then_inc(ones_ready, 1)
            dve.wait_ge(row_of_ready, len(row_of))
            for n in range(max(NG + LAG, NL) + 2):
                if n < NL:
                    prepare_lookup(n)
                g = n - 2 - LAG
                if 0 <= g < NG and g % 2 == 0:
                    copy_group(g, 0)
            dve.wait_ge(weights_loaded, 6 * 16)
            nc.vector.tensor_tensor(w_dense_sum[:, :], w_dense_2[:, 0, :], w_dense_2[:, 1, :], ALU.add)\
              .then_inc(w_dense_ready, 1)
            with dve.Fori(0, TILES - 1) as t:
                to_pairs(t)
                for h in range(5):
                    if h == 4:
                        finish(t)
                    if h == 0:
                        dve.wait_ge(dense_multiplied, HALVES * (t + 1))
                        copy_group(0, t + 1)
                    for g in WHERE:
                        if WHERE[g] == h and g % 2 == 0:
                            copy_group(g, t + 1)
            to_pairs(TILES - 1)
            finish(TILES - 1)


def kernel(**inputs):
    import concourse.bacc as bacc
    from concourse.bass_utils import run_bass_kernel_spmd

    nc = bacc.Bacc("TRN2", target_bir_lowering=False, num_devices=1)
    w1 = np.asarray(inputs["W_top1"])
    ids = np.asarray(inputs["ids"])
    laid_out = {
        "dense": inputs["r_dense_features"],
        "ids_gather": ids[:, GATHERED].reshape(TILES, ROWS, NGA).transpose(1, 0, 2).reshape(ROWS, TILES * NGA),
        "ids_lookup": ids[:, LOOKED_UP].T,
        **{f"tbl_{n}": inputs[f"tbl_{n}"] for n in range(TABLES)},
        "w_dense": np.concatenate([w1[:DIM], w1[DIM + PAIRS:]], axis=0),
        "w_pairs": w1[DIM:DIM + PAIRS][pair_rows()],
        "b1": inputs["b_top1"], "w2": inputs["W_top2"], "b2": inputs["b_top2"], "w3": inputs["W_top3"],
    }
    arrays, aps = {}, {}
    for name, a in laid_out.items():
        a = np.ascontiguousarray(a)
        arrays[f"in_{name}"] = a
        aps[name] = nc.dram_tensor(f"in_{name}", a.shape, mybir.dt.from_np(a.dtype), kind="ExternalInput").ap()
    out = nc.dram_tensor("out_y", (BATCH, 1), mybir.dt.float32, kind="ExternalOutput").ap()
    build(nc, aps["dense"], aps["ids_gather"], aps["ids_lookup"], [aps[f"tbl_{n}"] for n in range(TABLES)],
          aps["w_dense"], aps["w_pairs"], aps["b1"], aps["w2"], aps["b2"], aps["w3"], out)
    r = run_bass_kernel_spmd(nc, [arrays], core_ids=[0])
    return r.results[0]["out_y"]
```

```python
import numpy as np
import concourse.bass as bass
from concourse import mybir
from contextlib import ExitStack


TABLE_ROWS = [1250, 12500, 12500, 1000, 1250, 1250, 1250, 1250, 125000, 12500, 1250, 1250, 12500, 1250, 12500,
              1000, 1000, 12500, 12500, 1000, 12500, 1250, 1000, 1250, 1250, 1250]
TABLES = len(TABLE_ROWS)
FEATS = TABLES + 1
DIM = 128
BATCH = 512
ROWS = 128
TILES = BATCH // ROWS
H1, H2 = 512, 256
PAIRS = FEATS * (FEATS - 1) // 2

LOOKED_UP = [3, 15, 0, 4, 5, 16, 19, 22]
GATHERED = [n for n in range(TABLES) if n not in LOOKED_UP]
NL, NGA = len(LOOKED_UP), len(GATHERED)
GROUP = 4
DENSE_GROUP = 3
DENSE = NL + GROUP * DENSE_GROUP
ORDER = [n + 1 for n in LOOKED_UP + GATHERED]
ORDER.insert(DENSE, 0)

SHIFTS = FEATS // 2
CHUNKS = 3
CHUNK_F = FEATS // CHUNKS
CHUNK = CHUNK_F * SHIFTS

LP = 125
LP_MAIN = 120


def pair_rows():
    iu, ju = np.triu_indices(FEATS, k=1)
    row = {(int(a), int(b)): n for n, (a, b) in enumerate(zip(iu, ju))}
    rows = []
    for f in range(FEATS):
        for k in range(1, SHIFTS + 1):
            a, b = ORDER[f], ORDER[(f + k) % FEATS]
            rows.append(row[min(a, b), max(a, b)])
    return rows


def build(nc, dense, ids_gather, ids_lookup, tables, w_dense, w_pairs, b1, w2, b2, w3, out):
    fp32 = mybir.dt.float32
    fp32r = mybir.dt.float32r
    i32 = mybir.dt.int32
    ALU = mybir.AluOpType
    ACT = mybir.ActivationFunctionType

    Q = 32
    QUADS = ROWS // Q
    FIRST = NL
    GROUPS = [list(range(g, min(g + GROUP, FEATS - 1))) for g in range(FIRST, FEATS - 1, GROUP)] + [[FEATS - 1]]
    NG = len(GROUPS)
    BY_ACT, BY_DVE = [0, 1, 4], [2, 3, 5]
    assert sorted(BY_ACT + BY_DVE) == list(range(NG)) and DENSE_GROUP in BY_DVE
    TBUF = 4
    PBUF = 3
    NBUF = 3
    ACT_CHUNKS = 2
    WARM_START, WARM_LAYERS, WARM_GRAM = 14, 1, 2
    WHERE_FIRST = {0: -1, 1: -1, 2: 0, 3: 1, 4: 2, 5: 3}
    WHERE = {0: -1, 1: 1, 2: 2, 3: 3, 4: 4, 5: 4}
    AHEAD = 2
    AFTER = [min(g + 1, NL - 2) for g in range(NG)] + [NL - 2, NL - 1]
    K1 = H1 // 128
    WRAPPED = FEATS + SHIFTS
    TRANSPOSED = [(0, CHUNK_F + SHIFTS), (CHUNK_F + SHIFTS, FEATS), (FEATS, WRAPPED)]
    COUNTS = [TABLE_ROWS[n] // LP for n in LOOKED_UP]
    CMAX = max(COUNTS)
    assert all(c * LP == TABLE_ROWS[n] for c, n in zip(COUNTS, LOOKED_UP))

    ctx = ExitStack()
    with ctx:
        def sb(name, shape, dt=fp32):
            return ctx.enter_context(nc.sbuf_tensor(name, shape, dt))

        def ps(name, shape, dt=fp32):
            return ctx.enter_context(nc.psum_tensor(name, shape, dt))

        def sem(name):
            return ctx.enter_context(nc.semaphore(name))

        zeros = sb("zeros", [128, 512], mybir.dt.bfloat16)
        ones_row = sb("ones_row", [1, ROWS])
        one = sb("one", [LP, 1])
        identity = sb("identity", [128, 128])
        row_of = {c: sb(f"row_of{c}", [LP, c]) for c in sorted(set(COUNTS))}
        ids_now = sb("ids_now", [ROWS, 2, NGA], i32)
        w_dense_2 = sb("w_dense_2", [DIM, 2, H1])
        w_dense_sum = sb("w_dense_sum", [DIM, H1])
        w_pairs_sb = sb("w_pairs_sb", [CHUNK + 1, CHUNKS, H1])
        w2_sb = sb("w2_sb", [128, K1, H2])
        b2_sb = sb("b2_sb", [ROWS, H2])
        w3_sb = sb("w3_sb", [ROWS, H2])
        ids_wide = sb("ids_wide", [LP, NL, BATCH], i32)
        table = [sb(f"table{i}", [LP, CMAX, DIM]) for i in range(TBUF)]
        table_high = [sb(f"table_high{i}", [LP, CMAX, DIM], fp32r) for i in range(PBUF)]
        table_low = [sb(f"table_low{i}", [LP, CMAX, DIM], fp32r) for i in range(PBUF)]
        one_hot = [sb(f"one_hot{i}", [LP, CMAX, BATCH], fp32r) for i in range(NBUF)]
        distance = sb("distance", [LP, ACT_CHUNKS, BATCH])
        looked_up = sb("looked_up", [DIM, NL, BATCH])
        rows = sb("rows", [ROWS, FEATS - FIRST, DIM])
        cols = sb("cols", [DIM, FEATS, ROWS])
        inter = sb("inter", [ROWS, WRAPPED * 32])
        packed = sb("packed", [ROWS, PAIRS])
        pairs = sb("pairs", [CHUNK + 1, CHUNKS, ROWS])
        h1_cols = sb("h1_cols", [128, K1, ROWS])
        h2 = sb("h2", [ROWS, H2])
        h2_w3 = sb("h2_w3", [ROWS, H2])
        y = sb("y", [ROWS, 1])

        ps_cols = [ps(f"ps_cols{i}", [DIM, GROUP, ROWS]) for i in range(2)]
        ps_gram = ps("ps_gram", [128, 2, 512])
        bank = [ps(f"bank{i}", [128, 512]) for i in range(4)]
        ps_lookup = bank[0:2]
        ps_h1 = [bank[n][:, 0:ROWS] for n in range(K1)]
        ps_pairs = [bank[K1 - 1][0:CHUNK, 0:ROWS], ps_gram[0:CHUNK, 0, 0:ROWS], ps_gram[0:CHUNK, 1, 0:ROWS]]
        ps_h2 = bank[0][:, 0:H2]
        ps_pairs_last = [ps_cols[0][0:CHUNK, 0, :]] + ps_pairs[1:]
        ps_h2_last = ps_cols[1].rearrange("p g n -> p (g n)")[:, 0:H2]

        ids_loaded = [sem(f"ids_loaded{i}") for i in range(2)]
        ids_wide_loaded = [sem(f"ids_wide_loaded{i}") for i in range(NL)]
        table_loaded = [sem(f"table_loaded{i}") for i in range(NL)]
        weights_loaded = sem("weights_loaded")
        dense_loaded = sem("dense_loaded")
        group_gathered = [sem(f"group_gathered{g}") for g in range(NG)]
        groups_begun = sem("groups_begun")
        zeros_and_ones_ready = sem("zeros_and_ones_ready")
        identity_zeroed = sem("identity_zeroed")
        identity_ready = sem("identity_ready")
        row_of_ready = sem("row_of_ready")
        bias_ones_ready = sem("bias_ones_ready")
        gram_pads_ready = sem("gram_pads_ready")
        w_dense_ready = sem("w_dense_ready")
        high_ready = sem("high_ready")
        low_ready = sem("low_ready")
        one_hot_by_dve = sem("one_hot_by_dve")
        one_hots_by_act = sem("one_hots_by_act")
        distance_ready = sem("distance_ready")
        one_ready = sem("one_ready")
        lookup_summed = sem("lookup_summed")
        lookup_copied = sem("lookup_copied")
        group_transposed = sem("group_transposed")
        cols_by_dve = sem("cols_by_dve")
        cols_by_act = sem("cols_by_act")
        looked_up_in_cols = sem("looked_up_in_cols")
        dense_multiplied = sem("dense_multiplied")
        gram_ready = sem("gram_ready")
        inter_ready = sem("inter_ready")
        packed_ready = sem("packed_ready")
        pairs_transposed = sem("pairs_transposed")
        pairs_ready = sem("pairs_ready")
        h1_summed = sem("h1_summed")
        h1_ready = sem("h1_ready")
        h2_summed = sem("h2_summed")
        h2_biased = sem("h2_biased")
        y_ready = sem("y_ready")
        y_free = sem("y_free")
        out_stored = sem("out_stored")

        inter_at = inter[:, 0:1]

        def inter_pairs(c):
            return bass.AP(inter_at.tensor, inter_at.offset + 32 + 33 * CHUNK_F * c,
                           [list(inter_at.ap[0]), [33, CHUNK_F], [32, SHIFTS]])

        block = ctx.enter_context(nc.Block())

        @block.sync
        def _(sp):
            def load_ids(t):
                sp.dma_start(ids_now[:, t % 2, :], ids_gather[t * ROWS:(t + 1) * ROWS, :])\
                  .then_inc(ids_loaded[t % 2], 16)

            def load_dense(t):
                sp.dma_start(rows[:, DENSE - FIRST, :], dense[t * ROWS:(t + 1) * ROWS, :]).then_inc(dense_loaded, 16)

            def store(t):
                sp.wait_ge(y_ready, t + 1)
                sp.dma_start(out[t * ROWS:(t + 1) * ROWS, :], y[:, :]).then_inc(out_stored, 16)
                sp.wait_ge(out_stored, 16 * (t + 1))
                sp.sem_inc(y_free, 1)

            load_ids(0)
            for i in range(NL):
                c = COUNTS[i]
                if i >= TBUF:
                    sp.wait_ge(low_ready, i - TBUF + 1)
                sp.dma_start(ids_wide[:, i, :], ids_lookup[i:i + 1, :].to_broadcast([LP, BATCH]))\
                  .then_inc(ids_wide_loaded[i], 16)
                sp.dma_start(table[i % TBUF][0:LP_MAIN, 0:c, :],
                             tables[LOOKED_UP[i]][0:c * LP_MAIN, :].rearrange("(p c) d -> p c d", c=c))\
                  .then_inc(table_loaded[i], 16)
                sp.dma_start(table[i % TBUF][LP_MAIN:LP, 0:c, :],
                             tables[LOOKED_UP[i]][c * LP_MAIN:, :].rearrange("(p c) d -> p c d", c=c))\
                  .then_inc(table_loaded[i], 16)
                if i == 0:
                    load_ids(1)
                    load_dense(0)
            sp.dma_start(w_dense_2[:, :, :], w_dense.rearrange("(a p) n -> p a n", a=2)).then_inc(weights_loaded, 16)
            sp.dma_start(w_pairs_sb[0:CHUNK, :, :],
                         w_pairs.rearrange("(c p) n -> p c n", c=CHUNKS)).then_inc(weights_loaded, 16)
            sp.dma_start(w_pairs_sb[CHUNK:CHUNK + 1, CHUNKS - 1, :],
                         b1.rearrange("(a n) -> a n", a=1)).then_inc(weights_loaded, 16)
            sp.dma_start(w2_sb[:, :, :], w2.rearrange("(c p) n -> p c n", c=K1)).then_inc(weights_loaded, 16)
            sp.dma_start(b2_sb[:, :], b2.rearrange("(a n) -> a n", a=1).to_broadcast([ROWS, H2]))\
              .then_inc(weights_loaded, 16)
            sp.dma_start(w3_sb[:, :], w3.rearrange("n a -> a n").to_broadcast([ROWS, H2]))\
              .then_inc(weights_loaded, 16)
            sp.sem_inc(y_free, 1)
            for t in range(TILES):
                if t + 2 < TILES:
                    sp.wait_ge(group_transposed, NG + NG * (t + 1))
                    load_ids(t + 2)
                if t + 1 < TILES:
                    sp.wait_ge(group_transposed, NG + NG * t + DENSE_GROUP + 1)
                    load_dense(t + 1)
                if t > 0:
                    store(t - 1)
            store(TILES - 1)

        @block.gpsimd
        def _(pool):
            nc.gpsimd.memset(identity[:, :], 0.0).then_inc(identity_zeroed, 1)
            pool.wait_ge(identity_zeroed, 1)
            nc.gpsimd.affine_select(out=identity[:, :], in_=identity[:, :], compare_op=ALU.not_equal, fill=1.0,
                                    base=0, pattern=[[-1, 128]], channel_multiplier=1).then_inc(identity_ready, 1)
            for c, t in row_of.items():
                nc.gpsimd.iota(t[:, :], pattern=[[1, c]], base=0, channel_multiplier=c,
                               allow_small_or_imprecise_dtypes=True).then_inc(row_of_ready, 1)
            with pool.Fori(0, TILES // 2) as turn:
                for half in range(2):
                    t = turn * 2 + half
                    pool.wait_ge(ids_loaded[half], 16 * (turn + 1))
                    pool.sem_inc(groups_begun, 1)
                    for g, feats in enumerate(GROUPS):
                        pool.wait_ge(group_transposed, NG * t + g + 1)
                        pool.sem_inc(groups_begun, 1)
                        for f in feats:
                            if f == DENSE:
                                continue
                            n = f - FIRST - (f > DENSE)
                            nc.gpsimd.indirect_dma_start(
                                out=rows[:, f - FIRST, :], out_offset=None, in_=tables[GATHERED[n]][:, :],
                                in_offset=bass.IndirectOffsetOnAxis(ap=ids_now[:, half, n:n + 1], axis=0),
                            ).then_inc(group_gathered[g], 16)

        @block.tensor
        def _(pe):
            def keep_warm(n):
                for _ in range(n):
                    nc.tensor.matmul(bank[K1 - 1][:, :], zeros[:, 0:128], zeros[:, :], start=True, stop=True)

            def look_up(i):
                pe.wait_ge(high_ready, i + 1)
                pe.wait_ge(low_ready, i + 1)
                if i >= 2:
                    pe.wait_ge(lookup_copied, i - 1)
                for c in range(COUNTS[i]):
                    if c < COUNTS[i] - ACT_CHUNKS:
                        pe.wait_ge(one_hot_by_dve, sum(COUNTS[:i]) - i * ACT_CHUNKS + c + 1)
                    else:
                        pe.wait_ge(one_hots_by_act, i + 1)
                    for part in (table_high, table_low):
                        last = nc.tensor.matmul(ps_lookup[i % 2][:, :], part[i % PBUF][:, c, :],
                                                one_hot[i % NBUF][:, c, :],
                                                start=c == 0 and part is table_high,
                                                stop=c == COUNTS[i] - 1 and part is table_low)
                last.then_inc(lookup_summed, 1)

            def transpose_group(g, t):
                feats = GROUPS[g]
                if g == DENSE_GROUP:
                    pe.wait_ge(dense_loaded, 16 * (t + 1))
                    pe.wait_ge(group_gathered[g], 16 * (len(feats) - 1) * (t + 1))
                else:
                    pe.wait_ge(group_gathered[g], 16 * len(feats) * (t + 1))
                if g >= 2 or not isinstance(t, int) or t > 0:
                    before, tile = (g - 2, t) if g >= 2 else (max(x for x in range(NG) if x % 2 == g), t - 1)
                    copied, groups = (cols_by_act, BY_ACT) if before in BY_ACT else (cols_by_dve, BY_DVE)
                    pe.wait_ge(copied, len(groups) * tile + groups.index(before) + 1)
                for i, f in enumerate(feats):
                    last = nc.tensor.transpose(ps_cols[g % 2][:, i, :], rows[:, f - FIRST, :], identity[:, :])
                last.then_inc(group_transposed, 1)

            def gram(t):
                pe.wait_ge(cols_by_dve, len(BY_DVE) * (t + 1))
                pe.wait_ge(cols_by_act, len(BY_ACT) * (t + 1))
                pe.wait_ge(looked_up_in_cols, t + 2)
                for q in range(Q):
                    at = q % (Q // 2) * FEATS
                    for j in range(QUADS):
                        p = Q * j + q
                        last = nc.tensor.matmul(ps_gram[32 * j:32 * j + FEATS, q // (Q // 2), at:at + FEATS],
                                                cols[:, :, p], cols[:, :, p], start=True, stop=True,
                                                tile_position=(0, 32 * j))
                last.then_inc(gram_ready, 1)

            def layers(t, fill, last_tile=False):
                def transpose_pairs(c):
                    pe.wait_ge(packed_ready, CHUNKS * t + c + 1)
                    nc.tensor.transpose((ps_pairs_last if last_tile else ps_pairs)[c],
                                        packed[:, CHUNK * c:CHUNK * (c + 1)],
                                        identity[:, :]).then_inc(pairs_transposed, 1)

                def layer1_dense(n):
                    return nc.tensor.matmul(ps_h1[n], w_dense_sum[:, 128 * n:128 * (n + 1)], cols[:, DENSE, :],
                                            start=True, stop=False)

                def layer1(c, n):
                    k = CHUNK + (c == CHUNKS - 1)
                    return nc.tensor.matmul(ps_h1[n], w_pairs_sb[0:k, c, 128 * n:128 * (n + 1)], pairs[0:k, c, :],
                                            start=False, stop=c == CHUNKS - 1)

                pe.wait_ge(h2_biased, t + 1)
                for n in range(K1 - 1):
                    layer1_dense(n)
                if last_tile:
                    layer1_dense(K1 - 1)
                    nc.tensor.matmul(ps_h2_last, ones_row[:, :], b2_sb[0:1, :], start=True, stop=False)
                fill(0)
                transpose_pairs(0)
                fill(1)
                pe.wait_ge(pairs_ready, CHUNKS * t + 1)
                if not last_tile:
                    layer1_dense(K1 - 1).then_inc(dense_multiplied, 1)
                for n in range(K1):
                    layer1(0, n)
                    if n == 0:
                        transpose_pairs(1)
                        transpose_pairs(2)
                for c in range(1, CHUNKS):
                    pe.wait_ge(pairs_ready, CHUNKS * t + c + 1)
                    for n in range(K1):
                        last = layer1(c, n)
                        if c == CHUNKS - 1:
                            last.then_inc(h1_summed, 1)
                    if c == 1:
                        fill(2)
                fill(3)
                for n in range(K1):
                    pe.wait_ge(h1_ready, K1 * t + n + 1)
                    last = nc.tensor.matmul(ps_h2_last if last_tile else ps_h2, h1_cols[:, n, :], w2_sb[:, n, :],
                                            start=n == 0 and not last_tile, stop=n == K1 - 1)
                last.then_inc(h2_summed, 1)
                fill(4)

            pe.wait_ge(zeros_and_ones_ready, 2)
            keep_warm(WARM_START)
            pe.wait_ge(identity_ready, 1)
            pe.sem_inc(group_transposed, NG)
            for n in range(NL):
                look_up(n)
                for k in range(NG + AHEAD):
                    if AFTER[k] == n:
                        transpose_group(k % NG, k // NG)
            pe.wait_ge(gram_pads_ready, 1)
            pe.wait_ge(w_dense_ready, 1)

            def transpose_at(n, t, where):
                for g in where:
                    if where[g] == n:
                        transpose_group(g, t + 1)
                        if n == 4 and g == NG - 1:
                            keep_warm(WARM_GRAM)
                if n == 0 and where is WHERE:
                    keep_warm(WARM_LAYERS)

            gram(0)
            pe.wait_ge(lookup_copied, NL)
            layers(0, lambda n: transpose_at(n, 0, WHERE_FIRST))
            with pe.Fori(1, TILES - 1) as t:
                transpose_at(-1, t, WHERE)
                gram(t)
                layers(t, lambda n: transpose_at(n, t, WHERE))
            gram(TILES - 1)
            layers(TILES - 1, lambda n: None, last_tile=True)

        @block.scalar
        def _(act):
            def copy_group(g, t):
                act.wait_ge(group_transposed, NG * (t + 1) + g + 1)
                nc.scalar.activation(cols[:, GROUPS[g][0]:GROUPS[g][-1] + 1, :],
                                     ps_cols[g % 2][:, 0:len(GROUPS[g]), :], ACT.Copy).then_inc(cols_by_act, 1)

            def copy_lookup(i):
                act.wait_ge(lookup_summed, i + 1)
                nc.scalar.activation(looked_up[:, i, :], ps_lookup[i % 2][:, :], ACT.Copy).then_inc(lookup_copied, 1)

            def measure_distance(i):
                first = COUNTS[i] - ACT_CHUNKS
                act.wait_ge(ids_wide_loaded[i], 16)
                if i == 0:
                    act.wait_ge(row_of_ready, len(row_of))
                else:
                    act.wait_ge(one_hots_by_act, i)
                for n in range(ACT_CHUNKS):
                    nc.scalar.activation(distance[:, n, :], ids_wide[:, i, :], ACT.Square, scale=-1.0,
                                         bias=row_of[COUNTS[i]][:, first + n:first + n + 1])\
                      .then_inc(distance_ready, 1)

            def one_hots_by_distance(i):
                if i == 0:
                    act.wait_ge(one_ready, 1)
                if i >= NBUF:
                    act.wait_ge(lookup_summed, i - NBUF + 1)
                act.wait_ge(distance_ready, (i + 1) * ACT_CHUNKS)
                nc.scalar.activation(one_hot[i % NBUF][:, COUNTS[i] - ACT_CHUNKS:COUNTS[i], :], distance[:, :, :],
                                     ACT.Relu, scale=-1.0, bias=one[:, :]).then_inc(one_hots_by_act, 1)

            def place_looked_up(t):
                at = t * ROWS
                src = looked_up[:, :, bass.ds(at, ROWS)] if not isinstance(t, int) else looked_up[:, :, at:at + ROWS]
                nc.scalar.activation(cols[:, 0:NL, :], src, ACT.Copy).then_inc(looked_up_in_cols, 1)

            def layers(t, fill, last_tile=False):
                def pack(c):
                    act.wait_ge(inter_ready, len(TRANSPOSED) * t + (1 if c == 0 else len(TRANSPOSED)))
                    nc.scalar.activation(packed[:, CHUNK * c:CHUNK * (c + 1)].rearrange("p (f k) -> p f k", k=SHIFTS),
                                         inter_pairs(c), ACT.Copy).then_inc(packed_ready, 1)

                def copy_pairs(c):
                    act.wait_ge(pairs_transposed, CHUNKS * t + c + 1)
                    nc.scalar.activation(pairs[0:CHUNK, c, :], (ps_pairs_last if last_tile else ps_pairs)[c],
                                         ACT.Copy).then_inc(pairs_ready, 1)

                pack(0)
                fill(0)
                copy_pairs(0)
                pack(1)
                pack(2)
                fill(1)
                copy_pairs(1)
                copy_pairs(2)
                fill(2)
                for n in range(K1):
                    act.wait_ge(h1_summed, K1 * t + n + 1)
                    nc.scalar.activation(h1_cols[:, n, :], ps_h1[n], ACT.Relu).then_inc(h1_ready, 1)
                fill(3)
                fill(4)

            for n in range(NL + 2):
                if n < NL:
                    measure_distance(n)
                    act.wait_ge(table_loaded[n], 32)
                    if n >= PBUF:
                        act.wait_ge(lookup_summed, n - PBUF + 1)
                    nc.scalar.activation(table_high[n % PBUF][:, 0:COUNTS[n], :], table[n % TBUF][:, 0:COUNTS[n], :],
                                         ACT.Copy).then_inc(high_ready, 1)
                if n >= 2:
                    for g in BY_ACT:
                        if AFTER[g] == n - 2:
                            copy_group(g, 0)
                    if n - 2 == NL - 1:
                        act.wait_ge(lookup_copied, NL - 1)
                        nc.scalar.activation(cols[:, 0:NL - 1, :], looked_up[:, 0:NL - 1, 0:ROWS], ACT.Copy)\
                          .then_inc(looked_up_in_cols, 1)
                        act.wait_ge(lookup_summed, NL)
                        nc.scalar.activation(cols[:, NL - 1, :], ps_lookup[(NL - 1) % 2][:, 0:ROWS], ACT.Copy)\
                          .then_inc(looked_up_in_cols, 1)
                    copy_lookup(n - 2)
                if n < NL:
                    one_hots_by_distance(n)
            act.wait_ge(bias_ones_ready, 1)

            def fill(n, t, where):
                if n == 2:
                    place_looked_up(t + 1)
                for g in BY_ACT:
                    if where.get(g) == n:
                        copy_group(g, t + 1)

            def tile(t, where):
                act.wait_ge(gram_ready, t + 1)
                fill(-1, t, where)
                layers(t, lambda n: fill(n, t, where))

            tile(0, WHERE_FIRST)
            with act.Fori(1, TILES - 1) as t:
                tile(t, WHERE)
            layers(TILES - 1, lambda n: None, last_tile=True)

        @block.vector
        def _(dve):
            def copy_group(g, t):
                dve.wait_ge(group_transposed, NG * (t + 1) + g + 1)
                nc.vector.tensor_copy(cols[:, GROUPS[g][0]:GROUPS[g][-1] + 1, :],
                                      ps_cols[g % 2][:, 0:len(GROUPS[g]), :]).then_inc(cols_by_dve, 1)

            def prepare_lookup(i):
                c = COUNTS[i]
                """The one-hots of all but ScalarE's chunks, and the table's low part."""
                dve.wait_ge(ids_wide_loaded[i], 16)
                if i >= NBUF:
                    dve.wait_ge(lookup_summed, i - NBUF + 1)
                for n in range(c - ACT_CHUNKS):
                    nc.vector.tensor_scalar(one_hot[i % NBUF][:, n, :], ids_wide[:, i, :], row_of[c][:, n:n + 1], None,
                                            ALU.is_equal).then_inc(one_hot_by_dve, 1)
                dve.wait_ge(high_ready, i + 1)
                nc.vector.tensor_tensor(table_low[i % PBUF][:, 0:c, :], table[i % TBUF][:, 0:c, :],
                                        table_high[i % PBUF][:, 0:c, :].bitcast(fp32), ALU.subtract)\
                  .then_inc(low_ready, 1)

            def to_pairs(t):
                dve.wait_ge(gram_ready, t + 1)
                grams = ps_gram[:, :, 0:Q // 2 * FEATS].rearrange("p h (q m) -> p m h q", m=FEATS)
                for first, end in TRANSPOSED:
                    m, n = first % FEATS, end - first
                    nc.vector.transpose(
                        inter[:, 32 * first:32 * end].rearrange("p (m h f) -> p m h f", h=2, f=Q // 2),
                        grams[:, m:m + n, :, :]).then_inc(inter_ready, 1)

            def finish(t, last_tile=False):
                dve.wait_ge(h2_summed, t + 1)
                if not last_tile:
                    nc.vector.tensor_tensor(h2[:, :], ps_h2, b2_sb[:, :], ALU.add).then_inc(h2_biased, 1)
                    dve.wait_ge(h2_biased, t + 2)
                dve.wait_ge(y_free, t + 1)
                nc.vector.scalar_tensor_tensor(out=h2_w3[:, :], in0=ps_h2_last if last_tile else h2[:, :], scalar=0.0,
                                               in1=w3_sb[:, :], op0=ALU.max, op1=ALU.mult,
                                               accum_out=y[:, :]).then_inc(y_ready, 1)

            dve.sem_inc(h2_biased, 1)
            nc.vector.memset(zeros[:, :], 0.0).then_inc(zeros_and_ones_ready, 1)
            nc.vector.memset(ones_row[:, :], 1.0).then_inc(zeros_and_ones_ready, 1)
            nc.vector.memset(one[:, :], 1.0).then_inc(one_ready, 1)
            nc.vector.memset(ps_gram[:, :, :], 0.0).then_inc(gram_pads_ready, 1)
            nc.vector.memset(pairs[:, :, :], 1.0).then_inc(bias_ones_ready, 1)
            dve.wait_ge(row_of_ready, len(row_of))
            for n in range(NL + 2):
                if n < NL:
                    prepare_lookup(n)
                for g in BY_DVE:
                    if AFTER[g] == n - 2:
                        copy_group(g, 0)
            dve.wait_ge(weights_loaded, 6 * 16)
            nc.vector.tensor_tensor(w_dense_sum[:, :], w_dense_2[:, 0, :], w_dense_2[:, 1, :], ALU.add)\
              .then_inc(w_dense_ready, 1)

            def tile(t, where):
                to_pairs(t)
                for n in range(5):
                    if n == 4:
                        finish(t)
                    for g in BY_DVE:
                        if where[g] == n:
                            if g == DENSE_GROUP:
                                dve.wait_ge(dense_multiplied, t + 1)
                            copy_group(g, t + 1)

            tile(0, WHERE_FIRST)
            with dve.Fori(1, TILES - 1) as t:
                tile(t, WHERE)
            to_pairs(TILES - 1)
            finish(TILES - 1, last_tile=True)


def kernel(**inputs):
    import concourse.bacc as bacc
    from concourse.bass_utils import run_bass_kernel_spmd

    nc = bacc.Bacc("TRN2", target_bir_lowering=False, num_devices=1)
    w1 = np.asarray(inputs["W_top1"])
    ids = np.asarray(inputs["ids"])
    laid_out = {
        "dense": inputs["r_dense_features"],
        "ids_gather": ids[:, GATHERED],
        "ids_lookup": ids[:, LOOKED_UP].T,
        **{f"tbl_{n}": inputs[f"tbl_{n}"] for n in range(TABLES)},
        "w_dense": np.concatenate([w1[:DIM], w1[DIM + PAIRS:]], axis=0),
        "w_pairs": w1[DIM:DIM + PAIRS][pair_rows()],
        "b1": inputs["b_top1"], "w2": inputs["W_top2"], "b2": inputs["b_top2"], "w3": inputs["W_top3"],
    }
    arrays, aps = {}, {}
    for name, a in laid_out.items():
        a = np.ascontiguousarray(a)
        arrays[f"in_{name}"] = a
        aps[name] = nc.dram_tensor(f"in_{name}", a.shape, mybir.dt.from_np(a.dtype), kind="ExternalInput").ap()
    out = nc.dram_tensor("out_y", (BATCH, 1), mybir.dt.float32, kind="ExternalOutput").ap()
    build(nc, aps["dense"], aps["ids_gather"], aps["ids_lookup"], [aps[f"tbl_{n}"] for n in range(TABLES)],
          aps["w_dense"], aps["w_pairs"], aps["b1"], aps["w2"], aps["b2"], aps["w3"], out)
    r = run_bass_kernel_spmd(nc, [arrays], core_ids=[0])
    return r.results[0]["out_y"]
```
